# Optimizing a Trainium2 kernel written in Bass

```python
import numpy as np
import jax
import jax.numpy as jnp

def _softmax(x, axis=-1):
    return jax.nn.softmax(x, axis=axis)

def _gelu(x):
    return jax.nn.gelu(x, approximate=True)

def _silu(x):
    return jax.nn.silu(x)

def _sigmoid(x):
    return jax.nn.sigmoid(x)

def _layernorm(x, axis=-1, eps=1e-05):
    m = jnp.mean(x, axis=axis, keepdims=True)
    v = jnp.var(x, axis=axis, keepdims=True)
    return (x - m) / jnp.sqrt(v + eps)

def _scatter_add(tgt, idx, src, axis=0):
    return tgt.at[idx].add(src)

def _segment_sum(src, seg, n):
    return jax.ops.segment_sum(src, seg, n)
kernel_name = 'mk_dlrm_tower_d1_rec_r8_d69d74'

def setup_inputs(seed: int=0):
    np.random.seed(seed)
    _w = jnp.asarray

    def _rec_inputs():
        import jax
        import jax.numpy as jnp
        _tk = jax.random.key(seed)
        dense_ctx = jax.random.normal(jax.random.fold_in(_tk, 190), (1024, 16), jnp.float32)
        ids = jnp.stack([jax.random.randint(jax.random.fold_in(_tk, 200 + f), (1024,), 0, v, jnp.int32) for f, v in enumerate([12500, 1250, 125000, 1000, 1250, 12500, 12500, 1000, 1250, 12500, 1250, 1000, 1000, 125000, 12500, 1000, 1250, 12500, 1250, 12500, 1000, 125000, 1250, 1000, 12500, 1250, 1250, 1000, 1000, 1000, 1000, 1000])], axis=1)
        tbl_0 = 0.05 * jax.random.normal(jax.random.fold_in(_tk, 500 + 0), (12500, 64), jnp.float32)
        tbl_1 = 0.05 * jax.random.normal(jax.random.fold_in(_tk, 500 + 1), (1250, 64), jnp.float32)
        tbl_2 = 0.05 * jax.random.normal(jax.random.fold_in(_tk, 500 + 2), (125000, 64), jnp.float32)
        tbl_3 = 0.05 * jax.random.normal(jax.random.fold_in(_tk, 500 + 3), (1000, 64), jnp.float32)
        tbl_4 = 0.05 * jax.random.normal(jax.random.fold_in(_tk, 500 + 4), (1250, 64), jnp.float32)
        tbl_5 = 0.05 * jax.random.normal(jax.random.fold_in(_tk, 500 + 5), (12500, 64), jnp.float32)
        tbl_6 = 0.05 * jax.random.normal(jax.random.fold_in(_tk, 500 + 6), (12500, 64), jnp.float32)
        tbl_7 = 0.05 * jax.random.normal(jax.random.fold_in(_tk, 500 + 7), (1000, 64), jnp.float32)
        tbl_8 = 0.05 * jax.random.normal(jax.random.fold_in(_tk, 500 + 8), (1250, 64), jnp.float32)
        tbl_9 = 0.05 * jax.random.normal(jax.random.fold_in(_tk, 500 + 9), (12500, 64), jnp.float32)
        tbl_10 = 0.05 * jax.random.normal(jax.random.fold_in(_tk, 500 + 10), (1250, 64), jnp.float32)
        tbl_11 = 0.05 * jax.random.normal(jax.random.fold_in(_tk, 500 + 11), (1000, 64), jnp.float32)
        tbl_12 = 0.05 * jax.random.normal(jax.random.fold_in(_tk, 500 + 12), (1000, 64), jnp.float32)
        tbl_13 = 0.05 * jax.random.normal(jax.random.fold_in(_tk, 500 + 13), (125000, 64), jnp.float32)
        tbl_14 = 0.05 * jax.random.normal(jax.random.fold_in(_tk, 500 + 14), (12500, 64), jnp.float32)
        tbl_15 = 0.05 * jax.random.normal(jax.random.fold_in(_tk, 500 + 15), (1000, 64), jnp.float32)
        tbl_16 = 0.05 * jax.random.normal(jax.random.fold_in(_tk, 500 + 16), (1250, 64), jnp.float32)
        tbl_17 = 0.05 * jax.random.normal(jax.random.fold_in(_tk, 500 + 17), (12500, 64), jnp.float32)
        tbl_18 = 0.05 * jax.random.normal(jax.random.fold_in(_tk, 500 + 18), (1250, 64), jnp.float32)
        tbl_19 = 0.05 * jax.random.normal(jax.random.fold_in(_tk, 500 + 19), (12500, 64), jnp.float32)
        tbl_20 = 0.05 * jax.random.normal(jax.random.fold_in(_tk, 500 + 20), (1000, 64), jnp.float32)
        tbl_21 = 0.05 * jax.random.normal(jax.random.fold_in(_tk, 500 + 21), (125000, 64), jnp.float32)
        tbl_22 = 0.05 * jax.random.normal(jax.random.fold_in(_tk, 500 + 22), (1250, 64), jnp.float32)
        tbl_23 = 0.05 * jax.random.normal(jax.random.fold_in(_tk, 500 + 23), (1000, 64), jnp.float32)
        tbl_24 = 0.05 * jax.random.normal(jax.random.fold_in(_tk, 500 + 24), (12500, 64), jnp.float32)
        tbl_25 = 0.05 * jax.random.normal(jax.random.fold_in(_tk, 500 + 25), (1250, 64), jnp.float32)
        tbl_26 = 0.05 * jax.random.normal(jax.random.fold_in(_tk, 500 + 26), (1250, 64), jnp.float32)
        tbl_27 = 0.05 * jax.random.normal(jax.random.fold_in(_tk, 500 + 27), (1000, 64), jnp.float32)
        tbl_28 = 0.05 * jax.random.normal(jax.random.fold_in(_tk, 500 + 28), (1000, 64), jnp.float32)
        tbl_29 = 0.05 * jax.random.normal(jax.random.fold_in(_tk, 500 + 29), (1000, 64), jnp.float32)
        tbl_30 = 0.05 * jax.random.normal(jax.random.fold_in(_tk, 500 + 30), (1000, 64), jnp.float32)
        tbl_31 = 0.05 * jax.random.normal(jax.random.fold_in(_tk, 500 + 31), (1000, 64), jnp.float32)
        _rk = jax.random.fold_in(_tk, 7)
        W_top1 = 0.0693375 * jax.random.normal(jax.random.fold_in(_tk, 801), (208, 512), jnp.float32)
        W_top2 = 0.0441942 * jax.random.normal(jax.random.fold_in(_tk, 802), (512, 256), jnp.float32)
        W_top3 = 0.0625 * jax.random.normal(jax.random.fold_in(_tk, 803), (256, 1), jnp.float32)
        b_top1 = jnp.zeros((512,), jnp.float32)
        b_top2 = jnp.zeros((256,), jnp.float32)
        return (dense_ctx, ids, tbl_0, tbl_1, tbl_2, tbl_3, tbl_4, tbl_5, tbl_6, tbl_7, tbl_8, tbl_9, tbl_10, tbl_11, tbl_12, tbl_13, tbl_14, tbl_15, tbl_16, tbl_17, tbl_18, tbl_19, tbl_20, tbl_21, tbl_22, tbl_23, tbl_24, tbl_25, tbl_26, tbl_27, tbl_28, tbl_29, tbl_30, tbl_31, W_top1, b_top1, W_top2, b_top2, W_top3)
    dense_ctx, ids, tbl_0, tbl_1, tbl_2, tbl_3, tbl_4, tbl_5, tbl_6, tbl_7, tbl_8, tbl_9, tbl_10, tbl_11, tbl_12, tbl_13, tbl_14, tbl_15, tbl_16, tbl_17, tbl_18, tbl_19, tbl_20, tbl_21, tbl_22, tbl_23, tbl_24, tbl_25, tbl_26, tbl_27, tbl_28, tbl_29, tbl_30, tbl_31, W_top1, b_top1, W_top2, b_top2, W_top3 = _rec_inputs()

    def _L0_rec_setup():
        import jax, jax.numpy as jnp
        import numpy as np
        B, F_SIZE, DIM = (256, 32, 64)
        LAYER_SIZES = (128, 128)

        def _cin_forward(inputs, Ws, bs):
            batch, _, dim = inputs.shape
            x0 = inputs
            h = inputs
            finals = []
            n_layers = len(Ws)
            for i in range(n_layers):
                H = h.shape[1]
                M = x0.shape[1]
                z = jnp.einsum('bhd,bmd->bhmd', h, x0).reshape(batch, H * M, dim)
                out = jnp.einsum('bcd,oc->bod', z, Ws[i]) + bs[i][None, :, None]
                out = jax.nn.relu(out)
                size = Ws[i].shape[0]
                if i != n_layers - 1:
                    h = out[:, :size // 2, :]
                    finals.append(out[:, size // 2:, :])
                else:
                    finals.append(out)
            result = jnp.concatenate(finals, axis=1)
            return jnp.sum(result, axis=-1)
        key = jax.random.key(seed)
        k1, k2, k3 = jax.random.split(key, 3)
        inputs = jax.random.normal(k1, (B, F_SIZE, DIM), dtype=jnp.float32)
        W0 = jax.random.normal(k2, (128, F_SIZE * F_SIZE), dtype=jnp.float32) * 0.03
        b0 = jnp.zeros((128,), dtype=jnp.float32)
        W1 = jax.random.normal(k3, (128, 64 * F_SIZE), dtype=jnp.float32) * 0.03
        b1 = jnp.zeros((128,), dtype=jnp.float32)
        return {'inputs': inputs, 'W0': W0, 'b0': b0, 'W1': W1, 'b1': b1}
    _L0_rec_all = _L0_rec_setup()
    _L0_rec_in = {k: v for k, v in _L0_rec_all.items() if k in ('W0', 'b0', 'W1', 'b1')}
    del _L0_rec_all
    return {'dense_ctx': dense_ctx, 'ids': ids, 'tbl_0': tbl_0, 'tbl_1': tbl_1, 'tbl_2': tbl_2, 'tbl_3': tbl_3, 'tbl_4': tbl_4, 'tbl_5': tbl_5, 'tbl_6': tbl_6, 'tbl_7': tbl_7, 'tbl_8': tbl_8, 'tbl_9': tbl_9, 'tbl_10': tbl_10, 'tbl_11': tbl_11, 'tbl_12': tbl_12, 'tbl_13': tbl_13, 'tbl_14': tbl_14, 'tbl_15': tbl_15, 'tbl_16': tbl_16, 'tbl_17': tbl_17, 'tbl_18': tbl_18, 'tbl_19': tbl_19, 'tbl_20': tbl_20, 'tbl_21': tbl_21, 'tbl_22': tbl_22, 'tbl_23': tbl_23, 'tbl_24': tbl_24, 'tbl_25': tbl_25, 'tbl_26': tbl_26, 'tbl_27': tbl_27, 'tbl_28': tbl_28, 'tbl_29': tbl_29, 'tbl_30': tbl_30, 'tbl_31': tbl_31, 'W_top1': W_top1, 'b_top1': b_top1, 'W_top2': W_top2, 'b_top2': b_top2, 'W_top3': W_top3, 'L0_rec_W0': _L0_rec_in['W0'], 'L0_rec_b0': _L0_rec_in['b0'], 'L0_rec_W1': _L0_rec_in['W1'], 'L0_rec_b1': _L0_rec_in['b1']}

def reference(dense_ctx, ids, tbl_0, tbl_1, tbl_2, tbl_3, tbl_4, tbl_5, tbl_6, tbl_7, tbl_8, tbl_9, tbl_10, tbl_11, tbl_12, tbl_13, tbl_14, tbl_15, tbl_16, tbl_17, tbl_18, tbl_19, tbl_20, tbl_21, tbl_22, tbl_23, tbl_24, tbl_25, tbl_26, tbl_27, tbl_28, tbl_29, tbl_30, tbl_31, W_top1, b_top1, W_top2, b_top2, W_top3, L0_rec_W0, L0_rec_b0, L0_rec_W1, L0_rec_b1):
    import jax
    import jax.numpy as jnp

    def _L0_rec_ref(inputs, W0, b0, W1, b1):
        import jax, jax.numpy as jnp
        import numpy as np
        B, F_SIZE, DIM = (256, 32, 64)
        LAYER_SIZES = (128, 128)

        def _cin_forward(inputs, Ws, bs):
            batch, _, dim = inputs.shape
            x0 = inputs
            h = inputs
            finals = []
            n_layers = len(Ws)
            for i in range(n_layers):
                H = h.shape[1]
                M = x0.shape[1]
                z = jnp.einsum('bhd,bmd->bhmd', h, x0).reshape(batch, H * M, dim)
                out = jnp.einsum('bcd,oc->bod', z, Ws[i]) + bs[i][None, :, None]
                out = jax.nn.relu(out)
                size = Ws[i].shape[0]
                if i != n_layers - 1:
                    h = out[:, :size // 2, :]
                    finals.append(out[:, size // 2:, :])
                else:
                    finals.append(out)
            result = jnp.concatenate(finals, axis=1)
            return jnp.sum(result, axis=-1)
        return _cin_forward(inputs, (W0, W1), (b0, b1))
    e = jnp.stack([tbl_0[ids[:, 0]], tbl_1[ids[:, 1]], tbl_2[ids[:, 2]], tbl_3[ids[:, 3]], tbl_4[ids[:, 4]], tbl_5[ids[:, 5]], tbl_6[ids[:, 6]], tbl_7[ids[:, 7]], tbl_8[ids[:, 8]], tbl_9[ids[:, 9]], tbl_10[ids[:, 10]], tbl_11[ids[:, 11]], tbl_12[ids[:, 12]], tbl_13[ids[:, 13]], tbl_14[ids[:, 14]], tbl_15[ids[:, 15]], tbl_16[ids[:, 16]], tbl_17[ids[:, 17]], tbl_18[ids[:, 18]], tbl_19[ids[:, 19]], tbl_20[ids[:, 20]], tbl_21[ids[:, 21]], tbl_22[ids[:, 22]], tbl_23[ids[:, 23]], tbl_24[ids[:, 24]], tbl_25[ids[:, 25]], tbl_26[ids[:, 26]], tbl_27[ids[:, 27]], tbl_28[ids[:, 28]], tbl_29[ids[:, 29]], tbl_30[ids[:, 30]], tbl_31[ids[:, 31]]], axis=1)
    z = _L0_rec_ref(e, L0_rec_W0, L0_rec_b0, L0_rec_W1, L0_rec_b1)
    z = z.reshape(z.shape[0], -1)
    h = jnp.concatenate([z, dense_ctx], axis=1)
    h = jnp.maximum(h @ W_top1 + b_top1, 0.0)
    h = jnp.maximum(h @ W_top2 + b_top2, 0.0)
    y = h @ W_top3
    return y

_drawn_inputs = setup_inputs


def setup_inputs(seed=0):
    import zlib

    import numpy as np

    out = dict(_drawn_inputs(seed))
    spreads = {'b_top1': (0.0, 2.0),
     'b_top2': (0.0, 2.0),
     'L0_rec_b0': (0.0, 0.1),
     'L0_rec_b1': (0.0, 0.611)}
    factors = {'tbl_0': 8.0,
     'tbl_1': 8.0,
     'tbl_2': 8.0,
     'tbl_3': 8.0,
     'tbl_4': 8.0,
     'tbl_5': 8.0,
     'tbl_6': 8.0,
     'tbl_7': 8.0,
     'tbl_8': 8.0,
     'tbl_9': 8.0,
     'tbl_10': 8.0,
     'tbl_11': 8.0,
     'tbl_12': 8.0,
     'tbl_13': 8.0,
     'tbl_14': 8.0,
     'tbl_15': 8.0,
     'tbl_16': 8.0,
     'tbl_17': 8.0,
     'tbl_18': 8.0,
     'tbl_19': 8.0,
     'tbl_20': 8.0,
     'tbl_21': 8.0,
     'tbl_22': 8.0,
     'tbl_23': 8.0,
     'tbl_24': 8.0,
     'tbl_25': 8.0,
     'tbl_26': 8.0,
     'tbl_27': 8.0,
     'tbl_28': 8.0,
     'tbl_29': 8.0,
     'tbl_30': 8.0,
     'tbl_31': 8.0,
     'L0_rec_W0': 8.0,
     'L0_rec_W1': 7.99,
     'dense_ctx': 21.508}
    for name, (base, spread) in spreads.items():
        noise = np.random.default_rng([zlib.crc32(name.encode()), seed]).standard_normal(out[name].shape)
        drawn = base * np.exp(spread * noise) if base else spread * noise
        out[name] = jnp.asarray(drawn.astype(out[name].dtype))
    for name, factor in factors.items():
        out[name] = (out[name] * factor).astype(out[name].dtype)
    return out
```

```python
import numpy as np

import concourse.bass as bass
from concourse import mybir
from contextlib import ExitStack

FIELDS, DIM, BATCH, OUTS = 32, 64, 1024, 128
HID = OUTS // 2
GROUPS = 128 // FIELDS
CHUNK = 16
COLS = CHUNK * DIM
CHUNKS = BATCH // CHUNK
PER_GROUP = CHUNK // GROUPS
SHIFTS = FIELDS // GROUPS
FULL0 = FIELDS // 2 // GROUPS
REST0 = FIELDS // 2
TILES0 = FULL0 + 1
TILES1 = 2 * SHIFTS
EARLY1 = TILES1 // 2
PER_CHUNK = TILES0 + TILES1
RING = 7
BANK = 512
BANKS = COLS // BANK
T1, T2 = 512, 256
DENSE = 16


def dlrm_tower(nc, ids, table_base, tables, dense, w0_im, w0_mi, b0, w1, b1, wt1, bt1, wt2, bt2, wt3, out):
    f32, i32 = mybir.dt.float32, mybir.dt.int32
    ALU, ACT = mybir.AluOpType, mybir.ActivationFunctionType

    ctx = ExitStack()
    with ctx:
        def sb(name, shape, dt=f32):
            return ctx.enter_context(nc.sbuf_tensor(name, shape, dt))

        def ps(name, shape):
            return ctx.enter_context(nc.psum_tensor(name, shape, f32))

        def sem(name):
            return ctx.enter_context(nc.semaphore(name))

        x_dram = nc.dram_tensor("x_twice", [CHUNKS, 2, FIELDS, COLS], f32, kind="Internal").ap()

        ids_sb = sb("ids_sb", [128, CHUNKS * PER_GROUP], i32)
        base_sb = sb("base_sb", [128, 1], i32)
        rows_sb = [sb(f"rows_sb{p}", [128, PER_GROUP], i32) for p in range(2)]
        gath = [sb(f"gath{p}", [128, PER_GROUP * DIM]) for p in range(2)]
        x4 = [sb(f"x4_{p}", [128, COLS]) for p in range(2)]
        shifts = [sb(f"shifts{p}", [128, SHIFTS, COLS]) for p in range(2)]
        h4 = [sb(f"h4_{p}", [128, 2, COLS]) for p in range(2)]
        prod = [sb(f"prod{r}", [128, COLS]) for r in range(RING)]
        w0_sb = sb("w0_sb", [128, TILES0, OUTS])
        w0_mi_sb = sb("w0_mi_sb", [128, TILES0, OUTS])
        w1_sb = sb("w1_sb", [128, TILES1, OUTS])
        b0_sb = sb("b0_sb", [128, 1])
        b1_sb = sb("b1_sb", [128, 1])
        sum0 = sb("sum0", [OUTS - HID, BATCH])
        sum1 = sb("sum1", [128, BATCH])
        dense_sb = sb("dense_sb", [DENSE, BATCH])
        wt1_s0 = sb("wt1_s0", [OUTS - HID, T1])
        wt1_s1 = sb("wt1_s1", [OUTS, T1])
        wt1_d = sb("wt1_d", [DENSE, T1])
        bt1_sb = sb("bt1_sb", [128, T1 // 128])
        wt2_sb = sb("wt2_sb", [128, T1 // 128, T2])
        bt2_sb = sb("bt2_sb", [128, T2 // 128])
        wt3_sb = sb("wt3_sb", [128, T2 // 128])
        top1 = sb("top1", [128, T1 // 128, BATCH])
        top2 = sb("top2", [128, T2 // 128, BATCH])
        y_sb = sb("y_sb", [1, BATCH])

        acc0 = ps("acc0", [128, COLS])
        acc1 = [ps(f"acc1_{p}", [128, COLS]) for p in range(2)]
        acc_top = ps("acc_top", [128, BATCH])

        ids_in = sem("ids_in")
        cin_w_in = sem("cin_w_in")
        bias_in = sem("bias_in")
        top_w_in = sem("top_w_in")
        rows_ready = sem("rows_ready")
        w0_ready = sem("w0_ready")
        gathered = [sem(f"gathered{p}") for p in range(2)]
        stored = [sem(f"stored{p}") for p in range(2)]
        front_in = [sem(f"front_in{p}") for p in range(2)]
        back_in = [sem(f"back_in{p}") for p in range(2)]
        prod_ready = sem("prod_ready")
        prod_used = sem("prod_used")
        acc0_ready = sem("acc0_ready")
        acc0_free = sem("acc0_free")
        acc1_ready = sem("acc1_ready")
        acc1_free = sem("acc1_free")
        h_ready = sem("h_ready")
        top_ready = sem("top_ready")
        top_free = sem("top_free")
        y_out = sem("y_out")

        def number(c):
            return c[0] * 2 + c[1]

        def after(c):
            return (c[0], 1) if c[1] == 0 else (c[0] + 1, 0)

        LAST = CHUNKS - 1

        def at0(c, t):
            first = isinstance(c[0], int) and number(c) == 0
            return t if first else number(c) * PER_CHUNK + (TILES0 + EARLY1 - PER_CHUNK + t)

        def at1(c, j):
            last = isinstance(c[0], int) and number(c) == LAST
            return number(c) * PER_CHUNK + (TILES0 + j + (TILES0 if j >= EARLY1 and not last else 0))

        def slot(first, c, j):
            if isinstance(c[0], int):
                return first(c, j) % RING
            return first((3, c[1]), j) % RING

        def steps(engine, step, tail):
            for n in range(2):
                step((0, n), True)
            with engine.Fori(1, CHUNKS // 2 - 1) as half:
                for parity in range(2):
                    step((half, parity), False)
            step((CHUNKS // 2 - 1, 0), False)
            tail((CHUNKS // 2 - 1, 1))

        TOP1_GROUPS = T1 // 128 * (BATCH // BANK)
        TOP2_GROUPS = T2 // 128 * (BATCH // BANK)
        TOP_GROUPS = TOP1_GROUPS + TOP2_GROUPS + BATCH // BANK

        def top_groups():
            halves = [slice(n * BANK, (n + 1) * BANK) for n in range(BATCH // BANK)]
            for m in range(T1 // 128):
                out_rows = slice(m * 128, (m + 1) * 128)
                for h in halves:
                    yield (top1[:, m, h], [(wt1_s0[:, out_rows], sum0[:, h]),
                                           (wt1_s1[:, out_rows], sum1[:, h]),
                                           (wt1_d[:, out_rows], dense_sb[:, h])], ACT.Relu, bt1_sb[:, m:m + 1], 128)
            for m in range(T2 // 128):
                out_rows = slice(m * 128, (m + 1) * 128)
                for h in halves:
                    yield (top2[:, m, h], [(wt2_sb[:, k, out_rows], top1[:, k, h]) for k in range(T1 // 128)],
                           ACT.Relu, bt2_sb[:, m:m + 1], 128)
            for h in halves:
                yield (y_sb[:, h], [(wt3_sb[:, k:k + 1], top2[:, k, h]) for k in range(T2 // 128)],
                       ACT.Copy, None, 1)

        block = ctx.enter_context(nc.Block())

        @block.gpsimd
        def _(pool):
            pool.wait_ge(ids_in, 32)

            def gather(c, first):
                p = c[1]
                if not first:
                    pool.wait_ge(stored[p], c[0] * (16 * GROUPS))
                pool.tensor_tensor(rows_sb[p][:, :], ids_sb[:, bass.ds(number(c) * PER_GROUP, PER_GROUP)],
                                   base_sb[:, 0:1].to_broadcast([128, PER_GROUP]), ALU.add).then_inc(rows_ready, 1)
                pool.wait_ge(rows_ready, number(c) + 1)
                pool.nop(nofuse=True)
                for j in range(PER_GROUP):
                    pool.indirect_dma_start(
                        gath[p][:, j * DIM:(j + 1) * DIM], None, tables,
                        bass.IndirectOffsetOnAxis(ap=rows_sb[p][:, j:j + 1], axis=0),
                    ).then_inc(gathered[p], 16)

            steps(pool, gather, lambda c: gather(c, False))

        @block.sync
        def _(sp):
            sp.dma_start(ids_sb[:, :], ids).then_inc(ids_in, 16)
            sp.dma_start(base_sb[:, :], table_base).then_inc(ids_in, 16)
            sp.dma_start(w0_sb[:, :, :], w0_im).then_inc(cin_w_in, 16)
            sp.dma_start(w0_mi_sb[:, :, :], w0_mi).then_inc(cin_w_in, 16)
            sp.dma_start(w1_sb[:, :, :], w1).then_inc(cin_w_in, 16)
            sp.dma_start(b0_sb[:, :], b0).then_inc(bias_in, 16)
            sp.dma_start(b1_sb[:, :], b1).then_inc(bias_in, 16)

            def store(c):
                p = c[1]
                sp.wait_ge(gathered[p], c[0] * (16 * PER_GROUP) + 16 * PER_GROUP)
                w = PER_GROUP * DIM
                for g in range(GROUPS):
                    src = gath[p][g * FIELDS:(g + 1) * FIELDS, :].rearrange("f (a n) -> f a n", a=1)\
                        .to_broadcast([FIELDS, 2, w])
                    dst = x_dram[bass.ds(number(c), 1), :, :, g * w:(g + 1) * w].rearrange("a r f n -> (a f) r n")
                    sp.dma_start(dst, src).then_inc(stored[p], 16)

            def load(c, first):
                p = c[1]
                sp.wait_ge(stored[p], c[0] * (16 * GROUPS) + 16 * GROUPS)
                x = x_dram[bass.ds(number(c), 1), :, :, :].rearrange("a r f n -> (a r f) n")
                if not first:
                    sp.wait_ge(prod_ready, at1((c[0] - 1, p), 2 * TILES0 - 1) + 1)

                def group(g, lo, hi):
                    src = x[g + GROUPS * lo:g + GROUPS * lo + FIELDS, :]
                    rows = bass.AP(src.tensor, src.offset, [[COLS, FIELDS], [GROUPS * COLS, hi - lo], [1, COLS]])
                    return shifts[p][g * FIELDS:(g + 1) * FIELDS, lo:hi, :], rows

                for g in range(GROUPS):
                    sp.dma_start(x4[p][g * FIELDS:(g + 1) * FIELDS, :], x[0:FIELDS, :]).then_inc(front_in[p], 16)
                for g in range(GROUPS):
                    sp.dma_start(*group(g, 0, TILES0)).then_inc(front_in[p], 16)
                if not first:
                    sp.wait_ge(prod_ready, at1((c[0] - 1, p), TILES1 - 1) + 1)
                for g in range(GROUPS):
                    sp.dma_start(*group(g, TILES0, SHIFTS)).then_inc(back_in[p], 16)

            store((0, 0))

            def step(c, first):
                store(after(c))
                load(c, first)

            steps(sp, step, lambda c: load(c, False))
            sp.dma_start(dense_sb[:, :], dense).then_inc(top_w_in, 16)
            sp.dma_start(wt1_s0[:, :], wt1[0:OUTS - HID, :]).then_inc(top_w_in, 16)
            sp.dma_start(wt1_s1[:, :], wt1[OUTS - HID:2 * OUTS - HID, :]).then_inc(top_w_in, 16)
            sp.dma_start(wt1_d[:, :], wt1[2 * OUTS - HID:, :]).then_inc(top_w_in, 16)
            sp.dma_start(wt2_sb[:, :, :], wt2).then_inc(top_w_in, 16)
            sp.dma_start(wt3_sb[:, :], wt3).then_inc(top_w_in, 16)
            sp.dma_start(bt1_sb[:, :], bt1).then_inc(top_w_in, 16)
            sp.dma_start(bt2_sb[:, :], bt2).then_inc(top_w_in, 16)
            sp.wait_ge(top_free, TOP_GROUPS)
            sp.dma_start(out.rearrange("b a -> a b"), y_sb[:, :]).then_inc(y_out, 16)
            sp.wait_ge(y_out, 16)

        @block.vector
        def _(dve):
            dve.wait_ge(cin_w_in, 48)
            for lo, hi, t0, t1 in ((FIELDS, 2 * FIELDS, 0, 1), (2 * FIELDS, 128, 0, 1), (0, 128, 1, FULL0),
                                   (0, REST0, FULL0, TILES0)):
                part = w0_sb[lo:hi, t0:t1, :]
                dve.tensor_tensor(part, part, w0_mi_sb[lo:hi, t0:t1, :], ALU.add).then_inc(w0_ready, 1)

            def layer0(c, first):
                p = c[1]
                dve.wait_ge(front_in[p], c[0] * (16 * 2 * GROUPS) + 16 * 2 * GROUPS)
                for t in range(TILES0):
                    rows = 128 if t < FULL0 else REST0
                    if not first or at0(c, t) >= RING:
                        dve.wait_ge(prod_used, at0(c, t) - (RING - 1))
                    r = slot(at0, c, t)
                    dve.tensor_tensor(prod[r][0:rows, :], x4[p][0:rows, :], shifts[p][0:rows, t, :],
                                      ALU.mult).then_inc(prod_ready, 1)

            def layer1(c, first, lo, hi):
                p = c[1]
                for j in range(lo, hi):
                    if j == 0:
                        dve.wait_ge(h_ready, number(c) + 1)
                    if j == 2 * TILES0:
                        dve.wait_ge(back_in[p], c[0] * (16 * GROUPS) + 16 * GROUPS)
                    if not first or at1(c, j) >= RING:
                        dve.wait_ge(prod_used, at1(c, j) - (RING - 1))
                    r = slot(at1, c, j)
                    dve.tensor_tensor(prod[r][:, :], h4[p][:, j % 2, :], shifts[p][:, j // 2, :],
                                      ALU.mult).then_inc(prod_ready, 1)

            layer0((0, 0), True)

            def step(c, first):
                layer1(c, first, 0, EARLY1)
                layer0(after(c), first and c[1] == 0)
                layer1(c, first, EARLY1, TILES1)

            steps(dve, step, lambda c: layer1(c, False, 0, TILES1))

        @block.tensor
        def _(pe):
            pe.wait_ge(cin_w_in, 48)
            pe.wait_ge(w0_ready, 4)

            def layer0(c, first):
                if not first:
                    pe.wait_ge(acc0_free, number(c))
                for t in range(TILES0):
                    rows = 128 if t < FULL0 else REST0
                    pe.wait_ge(prod_ready, at0(c, t) + 1)
                    r = slot(at0, c, t)
                    for n in range(BANKS):
                        last = pe.matmul(acc0[:, n * BANK:(n + 1) * BANK], w0_sb[0:rows, t, :],
                                         prod[r][0:rows, n * BANK:(n + 1) * BANK],
                                         start=t == 0, stop=t == TILES0 - 1)
                    last.then_inc(prod_used, 1)

            def layer1(c, first, lo, hi):
                p = c[1]
                if lo == 0 and not first:
                    pe.wait_ge(acc1_free, number(c) - 1)
                for j in range(lo, hi):
                    pe.wait_ge(prod_ready, at1(c, j) + 1)
                    r = slot(at1, c, j)
                    for n in range(BANKS):
                        last = pe.matmul(acc1[p][:, n * BANK:(n + 1) * BANK], w1_sb[:, j, :],
                                         prod[r][:, n * BANK:(n + 1) * BANK],
                                         start=j == 0, stop=j == TILES1 - 1)
                    last.then_inc(prod_used, 1)

            layer0((0, 0), True)

            def step(c, first):
                layer1(c, first, 0, EARLY1)
                layer0(after(c), False)
                layer1(c, first, EARLY1, TILES1)

            steps(pe, step, lambda c: layer1(c, False, 0, TILES1))

            pe.wait_ge(top_w_in, 16 * 8)
            pe.wait_ge(acc0_free, CHUNKS)
            pe.wait_ge(acc1_free, CHUNKS)
            for n, (_, pairs, _, _, m) in enumerate(top_groups()):
                if n >= 2:
                    pe.wait_ge(top_free, n - 1)
                if n == TOP1_GROUPS or n == TOP1_GROUPS + TOP2_GROUPS:
                    pe.wait_ge(top_free, n)
                dst = acc_top[0:m, n % 2 * BANK:(n % 2 + 1) * BANK]
                for i, (w, x) in enumerate(pairs):
                    last = pe.matmul(dst, w, x, start=i == 0, stop=i == len(pairs) - 1)
                last.then_inc(top_ready, 1)

        @block.scalar
        def _(act):
            act.wait_ge(bias_in, 32)

            def sums(acc, bias, to, c, free):
                rows = to.shape[0]
                for b in range(CHUNK):
                    part = acc[0:rows, b * DIM:(b + 1) * DIM]
                    last = act.activation(part, part, ACT.Relu, bias=bias[0:rows, 0:1],
                                          accum_out=to[:, bass.ds(number(c) * CHUNK + b, 1)])
                last.then_inc(free, 1)

            def read0(c, first):
                p = c[1]
                act.wait_ge(prod_used, at0(c, TILES0 - 1) + 1)
                if not first:
                    act.wait_ge(prod_ready, at1((c[0] - 1, p), TILES1 - 1) + 1)
                for half in range(2):
                    lo = HID + half * FIELDS
                    for g in range(GROUPS):
                        last = act.activation(h4[p][g * FIELDS:(g + 1) * FIELDS, half, :],
                                              acc0[lo:lo + FIELDS, :], ACT.Relu, bias=b0_sb[lo:lo + FIELDS, 0:1])
                last.then_inc(h_ready, 1)
                sums(acc0, b0_sb, sum0, c, acc0_free)

            read0((0, 0), True)

            def step(c, first):
                read0(after(c), first and c[1] == 0)
                act.wait_ge(prod_used, at1(c, TILES1 - 1) + 1)
                sums(acc1[c[1]], b1_sb, sum1, c, acc1_free)

            def tail(c):
                act.wait_ge(prod_used, at1(c, TILES1 - 1) + 1)
                sums(acc1[c[1]], b1_sb, sum1, c, acc1_free)

            steps(act, step, tail)
            act.wait_ge(top_w_in, 16 * 8)
            for n, (to, _, func, bias, m) in enumerate(top_groups()):
                act.wait_ge(top_ready, n + 1)
                src = acc_top[0:m, n % 2 * BANK:(n % 2 + 1) * BANK]
                if bias is None:
                    act.activation(to, src, func).then_inc(top_free, 1)
                else:
                    act.activation(to, src, func, bias=bias).then_inc(top_free, 1)


def kernel(**inputs):
    import concourse.bacc as bacc
    from concourse.bass_utils import run_bass_kernel_spmd

    a = {k: np.asarray(v) for k, v in inputs.items()}
    names = [f"tbl_{f}" for f in range(FIELDS)]
    tables = np.concatenate([a[n] for n in names], axis=0)
    starts = np.cumsum([0] + [a[n].shape[0] for n in names[:-1]]).astype(np.int32)

    ids = a["ids"].reshape(CHUNKS, GROUPS, PER_GROUP, FIELDS).transpose(1, 3, 0, 2).reshape(128, -1)
    base = np.tile(starts, GROUPS).reshape(128, 1)

    i = np.arange(FIELDS)
    order = np.r_[HID:OUTS, 0:HID]
    w0 = a["L0_rec_W0"].reshape(OUTS, FIELDS, FIELDS)[order]
    w1 = a["L0_rec_W1"].reshape(OUTS, 2, FIELDS, FIELDS)

    def tile0(w, swap):
        t = np.empty((GROUPS, FIELDS, TILES0, OUTS), w.dtype)
        for s in range(GROUPS * TILES0):
            m = (i + s) % FIELDS
            t[s % GROUPS, :, s // GROUPS, :] = (w[:, m, i] if swap else w[:, i, m]).T
        return t.reshape(128, TILES0, OUTS)

    t1 = np.empty((GROUPS, FIELDS, SHIFTS, 2, OUTS), w1.dtype)
    for s in range(FIELDS):
        for half in range(2):
            t1[s % GROUPS, :, s // GROUPS, half, :] = w1[:, half, i, (i + s) % FIELDS].T

    arrays = {
        "ids": ids, "table_base": base, "tables": tables, "dense": a["dense_ctx"].T,
        "w0_im": tile0(w0, False), "w0_mi": tile0(w0, True), "b0": a["L0_rec_b0"][order].reshape(128, 1),
        "w1": t1.reshape(128, TILES1, OUTS), "b1": a["L0_rec_b1"].reshape(128, 1),
        "wt1": a["W_top1"], "bt1": a["b_top1"].reshape(-1, 128).T,
        "wt2": a["W_top2"].reshape(-1, 128, T2).transpose(1, 0, 2), "bt2": a["b_top2"].reshape(-1, 128).T,
        "wt3": a["W_top3"].reshape(-1, 128).T,
    }
    nc = bacc.Bacc("TRN2", target_bir_lowering=False, num_devices=1)
    arrays = {f"in_{k}": np.ascontiguousarray(v) for k, v in arrays.items()}
    args = [nc.dram_tensor(k, v.shape, mybir.dt.from_np(v.dtype), kind="ExternalInput").ap()
            for k, v in arrays.items()]
    out = nc.dram_tensor("out_y", (BATCH, 1), mybir.dt.float32, kind="ExternalOutput").ap()
    dlrm_tower(nc, *args, out)
    r = run_bass_kernel_spmd(nc, [arrays], core_ids=[0])
    return r.results[0]["out_y"]
```

```python
import numpy as np

import concourse.bass as bass
from concourse import mybir
from contextlib import ExitStack

FIELDS, DIM, BATCH, OUTS = 32, 64, 1024, 128
HID = OUTS // 2
GROUPS = 128 // FIELDS
CHUNK = 16
COLS = CHUNK * DIM
CHUNKS = BATCH // CHUNK
PER_GROUP = CHUNK // GROUPS
SHIFTS = FIELDS // GROUPS
FULL0 = FIELDS // 2 // GROUPS
TILES1 = 2 * SHIFTS
PAIR = 2
L0 = [("l0", u) for u in range(FULL0 // PAIR)] + ["rest"]
L1 = [("l1", u) for u in range(SHIFTS)]
FRONT = FULL0 + 1
EARLY = 2
SPLIT = [("l1", 1), ("l0", 1), ("l1", 2)]
SUMS_EARLY = 6
RING = 5
PARTS = 2
BANK = 512
BANKS = COLS // BANK
T1, T2 = 512, 256
DENSE = 16
FEATS0 = OUTS - HID


def dlrm_tower(nc, ids, table_base, tables, dense, w0_im, w0_mi, w0_rest, b0, w1, b1,
               wt1, bt1, wt2, bt2, wt3, out):
    f32, f32r, i32 = mybir.dt.float32, mybir.dt.float32r, mybir.dt.int32
    ALU, ACT = mybir.AluOpType, mybir.ActivationFunctionType

    ctx = ExitStack()
    with ctx:
        def sb(name, shape, dt=f32):
            return ctx.enter_context(nc.sbuf_tensor(name, shape, dt))

        def ps(name, shape):
            return ctx.enter_context(nc.psum_tensor(name, shape, f32))

        def sem(name):
            return ctx.enter_context(nc.semaphore(name))

        x_dram = nc.dram_tensor("x_twice", [CHUNKS, 2, FIELDS, COLS], f32, kind="Internal").ap()

        ids_sb = sb("ids_sb", [128, CHUNKS * PER_GROUP], i32)
        base_sb = sb("base_sb", [128, 1], i32)
        rows_sb = [sb(f"rows_sb{p}", [128, PER_GROUP], i32) for p in range(2)]
        gath = [sb(f"gath{p}", [128, PER_GROUP * DIM]) for p in range(2)]
        x4 = [sb(f"x4_{p}", [128, COLS]) for p in range(2)]
        shifts = [sb(f"shifts{p}", [128, SHIFTS, COLS]) for p in range(2)]
        h4 = [sb(f"h4_{p}", [128, 2, COLS]) for p in range(2)]
        prod = [sb(f"prod{r}", [128, PAIR, COLS]) for r in range(RING)]
        high = [sb(f"high{r}", [128, PAIR, COLS], f32r) for r in range(PARTS)]
        low = [sb(f"low{r}", [128, PAIR, COLS], f32r) for r in range(PARTS)]
        rest = sb("rest", [FIELDS, COLS])
        rest_parts = sb("rest_parts", [3 * FIELDS, COLS], f32r)
        w0_sb = sb("w0_sb", [128, FULL0, OUTS])
        w0_mi_sb = sb("w0_mi_sb", [128, FULL0, OUTS])
        w0_rest_sb = sb("w0_rest_sb", [FIELDS, OUTS])
        w0_rest_parts = sb("w0_rest_parts", [3 * FIELDS, OUTS], f32r)
        w1_sb = sb("w1_sb", [128, TILES1, OUTS])
        w_high = sb("w_high", [128, len(SPLIT) * PAIR, OUTS], f32r)
        w_low = sb("w_low", [128, len(SPLIT) * PAIR, OUTS], f32r)
        b0_sb = sb("b0_sb", [128, 1])
        b1_sb = sb("b1_sb", [128, 1])
        feats0 = sb("feats0", [FEATS0 + DENSE, BATCH])
        feats1 = sb("feats1", [OUTS, BATCH])
        wt1_0 = sb("wt1_0", [FEATS0 + DENSE, T1])
        wt1_1 = sb("wt1_1", [OUTS, T1])
        bt1_sb = sb("bt1_sb", [128, T1 // 128])
        wt2_sb = sb("wt2_sb", [128, T1 // 128, T2])
        bt2_sb = sb("bt2_sb", [128, T2 // 128])
        wt3_sb = sb("wt3_sb", [128, T2 // 128])
        assert BATCH == COLS and T1 // 128 + T2 // 128 < SHIFTS
        top1 = shifts[0][:, 0:T1 // 128, :]
        top2 = shifts[0][:, T1 // 128:T1 // 128 + T2 // 128, :]
        y_sb = shifts[0][0:1, SHIFTS - 1, :]

        acc0 = ps("acc0", [128, COLS])
        acc1 = [ps(f"acc1_{p}", [128, COLS]) for p in range(2)]
        acc_top = [ps(f"acc_top{n}", [128, BANK]) for n in range(2)]

        ids_in = sem("ids_in")
        w0_in = sem("w0_in")
        w1_in = sem("w1_in")
        bias_in = sem("bias_in")
        top_w_in = sem("top_w_in")
        rows_ready = sem("rows_ready")
        w0_ready = sem("w0_ready")
        w_high_ready = sem("w_high_ready")
        w_low_ready = sem("w_low_ready")
        gathered = [sem(f"gathered{p}") for p in range(2)]
        stored = [sem(f"stored{p}") for p in range(2)]
        start_in = sem("start_in")
        front_in = [sem(f"front_in{p}") for p in range(2)]
        back_in = [sem(f"back_in{p}") for p in range(2)]
        unit_made = sem("unit_made")
        high_made = sem("high_made")
        low_made = sem("low_made")
        unit_used = sem("unit_used")
        acc0_free = sem("acc0_free")
        acc1_free = sem("acc1_free")
        h_ready = sem("h_ready")
        h1_ready = sem("h1_ready")
        top_ready = sem("top_ready")
        top_free = sem("top_free")
        y_out = sem("y_out")

        def number(c):
            return c[0] * 2 + c[1]

        def after(c):
            return (c[0], 1) if c[1] == 0 else (c[0] + 1, 0)

        def before(c):
            return (c[0], 0) if c[1] == 1 else (c[0] - 1, 1)

        order = [(0, u) for u in L0]
        for k in range(CHUNKS):
            order += [(k, u) for u in L1[:EARLY]]
            order += [(k + 1, u) for u in L0] if k + 1 < CHUNKS else []
            order += [(k, u) for u in L1[EARLY:]]
        pairs = [x for x in order if x[1] != "rest"]
        split = [x for x in order if x[1] in SPLIT or x[1] == "rest"]
        split_pairs = [x for x in order if x[1] in SPLIT]

        def count(units, c, unit, back=0):
            per = sum(1 for x in units if x[0] == 8)
            if isinstance(c[0], int):
                return units.index((number(c) - back, unit)) + 1
            k = 8 + c[1]
            return number(c) * per + (units.index((k - back, unit)) + 1 - k * per)

        def place(units, n, c, unit):
            k = number(c) if isinstance(c[0], int) else 8 + c[1]
            at = units.index((k, unit))
            return at % n, (k - units[at - n][0], units[at - n][1]) if at >= n else None

        def steps(engine, step, tail):
            for n in range(2):
                step((0, n))
            with engine.Fori(1, CHUNKS // 2 - 1) as half:
                for parity in range(2):
                    step((half, parity))
            step((CHUNKS // 2 - 1, 0))
            tail((CHUNKS // 2 - 1, 1))

        def is_first(c):
            return isinstance(c[0], int) and number(c) < 2

        def top_groups():
            halves = [slice(n * BANK, (n + 1) * BANK) for n in range(BATCH // BANK)]
            for h in halves:
                for m in range(T1 // 128):
                    cols = slice(m * 128, (m + 1) * 128)
                    yield (top1[:, m, h], [(wt1_0[:, cols], feats0[:, h]), (wt1_1[:, cols], feats1[:, h])],
                           ACT.Relu, bt1_sb[:, m:m + 1], 128)
            for h in halves:
                for m in range(T2 // 128):
                    cols = slice(m * 128, (m + 1) * 128)
                    yield (top2[:, m, h], [(wt2_sb[:, k, cols], top1[:, k, h]) for k in range(T1 // 128)],
                           ACT.Relu, bt2_sb[:, m:m + 1], 128)
            for h in halves:
                yield (y_sb[:, h], [(wt3_sb[:, k:k + 1], top2[:, k, h]) for k in range(T2 // 128)],
                       ACT.Copy, None, 1)

        HALVES = BATCH // BANK
        TOP1_GROUPS, TOP2_GROUPS = T1 // 128 * HALVES, T2 // 128 * HALVES
        TOP_GROUPS = TOP1_GROUPS + TOP2_GROUPS + HALVES

        block = ctx.enter_context(nc.Block())

        @block.gpsimd
        def _(pool):
            pool.wait_ge(ids_in, 32)

            def gather(c):
                p = c[1]
                if not is_first(c):
                    pool.wait_ge(stored[p], c[0] * (16 * GROUPS))
                pool.tensor_tensor(rows_sb[p][:, :], ids_sb[:, bass.ds(number(c) * PER_GROUP, PER_GROUP)],
                                   base_sb[:, 0:1].to_broadcast([128, PER_GROUP]), ALU.add).then_inc(rows_ready, 1)
                pool.wait_ge(rows_ready, number(c) + 1)
                pool.nop(nofuse=True)
                for j in range(PER_GROUP):
                    pool.indirect_dma_start(
                        gath[p][:, j * DIM:(j + 1) * DIM], None, tables,
                        bass.IndirectOffsetOnAxis(ap=rows_sb[p][:, j:j + 1], axis=0),
                    ).then_inc(gathered[p], 16)

            steps(pool, gather, gather)

        @block.sync
        def _(sp):
            sp.dma_start(ids_sb[:, :], ids).then_inc(ids_in, 16)
            sp.dma_start(base_sb[:, :], table_base).then_inc(ids_in, 16)
            sp.dma_start(feats0[FEATS0:FEATS0 + DENSE, :], dense).then_inc(top_w_in, 16)

            def store(c):
                p = c[1]
                sp.wait_ge(gathered[p], c[0] * (16 * PER_GROUP) + 16 * PER_GROUP)
                w = PER_GROUP * DIM
                for g in range(GROUPS):
                    src = gath[p][g * FIELDS:(g + 1) * FIELDS, :].rearrange("f (a n) -> f a n", a=1)\
                        .to_broadcast([FIELDS, 2, w])
                    dst = x_dram[bass.ds(number(c), 1), :, :, g * w:(g + 1) * w].rearrange("a r f n -> (a f) r n")
                    sp.dma_start(dst, src).then_inc(stored[p], 16)

            def load(c):
                p = c[1]
                sp.wait_ge(stored[p], c[0] * (16 * GROUPS) + 16 * GROUPS)
                x = x_dram[bass.ds(number(c), 1), :, :, :].rearrange("a r f n -> (a r f) n")

                def shift_rows(g, lo, hi):
                    src = x[g + GROUPS * lo:g + GROUPS * lo + FIELDS, :]
                    rows = bass.AP(src.tensor, src.offset, [[COLS, FIELDS], [GROUPS * COLS, hi - lo], [1, COLS]])
                    return shifts[p][g * FIELDS:(g + 1) * FIELDS, lo:hi, :], rows

                if not is_first(c):
                    sp.wait_ge(unit_made, count(order, c, ("l1", FRONT - 1), back=2))
                zero = isinstance(c[0], int) and number(c) == 0
                for g in range(GROUPS):
                    sp.dma_start(x4[p][g * FIELDS:(g + 1) * FIELDS, :], x[0:FIELDS, :])\
                        .then_inc(start_in if zero else front_in[p], 16)
                if zero:
                    for lo, hi, done in ((0, PAIR, start_in), (PAIR, FULL0, front_in[p]), (FULL0, FRONT, front_in[p])):
                        for g in range(GROUPS):
                            sp.dma_start(*shift_rows(g, lo, hi)).then_inc(done, 16)
                else:
                    for g in range(GROUPS):
                        sp.dma_start(*shift_rows(g, 0, FRONT)).then_inc(front_in[p], 16)
                if not is_first(c):
                    sp.wait_ge(unit_made, count(order, c, L1[-1], back=2))
                for g in range(GROUPS):
                    sp.dma_start(*shift_rows(g, FRONT, SHIFTS)).then_inc(back_in[p], 16)

            store((0, 0))
            load((0, 0))

            def step(c):
                store(after(c))
                if not (isinstance(c[0], int) and number(c) == 0):
                    load(c)

            steps(sp, step, load)
            sp.dma_start(wt1_0[0:FEATS0, :], wt1[0:FEATS0, :]).then_inc(top_w_in, 16)
            sp.dma_start(wt1_0[FEATS0:FEATS0 + DENSE, :], wt1[FEATS0 + OUTS:, :]).then_inc(top_w_in, 16)
            sp.dma_start(wt1_1[:, :], wt1[FEATS0:FEATS0 + OUTS, :]).then_inc(top_w_in, 16)
            sp.dma_start(wt2_sb[:, :, :], wt2).then_inc(top_w_in, 16)
            sp.dma_start(wt3_sb[:, :], wt3).then_inc(top_w_in, 16)
            sp.dma_start(bt1_sb[:, :], bt1).then_inc(top_w_in, 16)
            sp.dma_start(bt2_sb[:, :], bt2).then_inc(top_w_in, 16)
            sp.wait_ge(top_free, TOP_GROUPS)
            sp.dma_start(out.rearrange("b a -> a b"), y_sb).then_inc(y_out, 16)
            sp.wait_ge(y_out, 16)

        @block.vector
        def _(dve):
            def product(c, unit):
                p = c[1]
                kind, u = unit
                zero = isinstance(c[0], int) and number(c) == 0
                if kind == "l0" and zero and u == 0:
                    dve.wait_ge(start_in, 16 * 2 * GROUPS)
                elif kind == "l0" and u == (1 if zero else 0):
                    dve.wait_ge(front_in[p], c[0] * (16 * 2 * GROUPS) + 16 * 2 * GROUPS)
                if kind == "l1" and u == 0:
                    dve.wait_ge(h_ready, number(c) + 1)
                if kind == "l1" and u == FRONT:
                    dve.wait_ge(back_in[p], c[0] * (16 * GROUPS) + 16 * GROUPS)
                slot, last = place(pairs, RING, c, unit)
                if last and last[1] in SPLIT:
                    dve.wait_ge(low_made, count(split, c, last[1], last[0]))
                elif last:
                    dve.wait_ge(unit_used, count(order, c, last[1], last[0]))
                if kind == "l0":
                    a = x4[p][:, :].rearrange("p (a n) -> p a n", a=1).to_broadcast([128, PAIR, COLS])
                    b = shifts[p][:, u * PAIR:(u + 1) * PAIR, :]
                else:
                    a = h4[p][:, :, :]
                    b = shifts[p][:, u:u + 1, :].to_broadcast([128, PAIR, COLS])
                dve.tensor_tensor(prod[slot][:, :, :], a, b, ALU.mult).then_inc(unit_made, 1)

            def low_part(c, unit):
                dve.wait_ge(high_made, count(split, c, unit))
                slot, _ = place(pairs, RING, c, unit)
                r, _ = place(split_pairs, PARTS, c, unit)
                dve.tensor_tensor(low[r][:, :, :], prod[slot][:, :, :], high[r][:, :, :].bitcast(f32),
                                  ALU.subtract).then_inc(low_made, 1)

            def product_rest(c):
                p = c[1]
                if not (isinstance(c[0], int) and number(c) == 0):
                    dve.wait_ge(low_made, count(split, c, "rest", 1))
                dve.tensor_tensor(rest[:, :], x4[p][0:FIELDS, :], shifts[p][0:FIELDS, FULL0, :], ALU.mult)\
                    .then_inc(unit_made, 1)

            def low_rest(c):
                dve.wait_ge(high_made, count(split, c, "rest"))
                dve.tensor_tensor(rest_parts[2 * FIELDS:, :], rest[:, :], rest_parts[0:FIELDS, :].bitcast(f32),
                                  ALU.subtract).then_inc(low_made, 1)

            dve.wait_ge(w0_in, 48)
            for lo, hi, t0, t1 in ((FIELDS, 2 * FIELDS, 0, 1), (2 * FIELDS, 128, 0, 1), (0, 128, 1, FULL0)):
                part = w0_sb[lo:hi, t0:t1, :]
                dve.tensor_tensor(part, part, w0_mi_sb[lo:hi, t0:t1, :], ALU.add).then_inc(w0_ready, 1)
            dve.wait_ge(w_high_ready, 1)
            dve.tensor_tensor(w0_rest_parts[FIELDS:2 * FIELDS, :], w0_rest_sb[:, :],
                              w0_rest_parts[0:FIELDS, :].bitcast(f32), ALU.subtract).then_inc(w_low_ready, 1)
            for n, (kind, u) in enumerate(SPLIT):
                w = (w0_sb if kind == "l0" else w1_sb)[:, u * PAIR:(u + 1) * PAIR, :]
                cols = slice(n * PAIR, (n + 1) * PAIR)
                dve.wait_ge(w_high_ready, n + 2)
                dve.tensor_tensor(w_low[:, cols, :], w, w_high[:, cols, :].bitcast(f32), ALU.subtract)\
                    .then_inc(w_low_ready, 1)
            product((0, 0), ("l0", 0))
            product((0, 0), ("l0", 1))
            product_rest((0, 0))
            low_part((0, 0), ("l0", 1))
            low_rest((0, 0))
            dve.wait_ge(bias_in, 32)
            dve.wait_ge(unit_used, count(order, (0, 0), "rest"))
            for g in range(GROUPS):
                dve.tensor_scalar(h4[0][g * FIELDS:(g + 1) * FIELDS, 1, :], acc0[OUTS - FIELDS:OUTS, :],
                                  b0_sb[OUTS - FIELDS:OUTS, 0:1], 0.0, ALU.add, ALU.max).then_inc(h1_ready, 1)
            dve.wait_ge(h1_ready, GROUPS)

            def step(c):
                product(c, ("l1", 0))
                product(c, ("l1", 1))
                product(after(c), ("l0", 0))
                low_part(c, ("l1", 1))
                product(after(c), ("l0", 1))
                product_rest(after(c))
                product(c, ("l1", 2))
                low_part(after(c), ("l0", 1))
                low_rest(after(c))
                low_part(c, ("l1", 2))
                for u in range(3, SHIFTS):
                    product(c, ("l1", u))

            def tail(c):
                product(c, ("l1", 0))
                product(c, ("l1", 1))
                product(c, ("l1", 2))
                low_part(c, ("l1", 1))
                product(c, ("l1", 3))
                low_part(c, ("l1", 2))
                for u in range(4, SHIFTS):
                    product(c, ("l1", u))

            steps(dve, step, tail)

        @block.tensor
        def _(pe):
            pe.wait_ge(w0_in, 48)
            pe.wait_ge(w1_in, 16)
            pe.wait_ge(w0_ready, 3)
            pe.wait_ge(w_low_ready, 1 + len(SPLIT))

            def banks(acc, w, x, start=False, stop=False):
                for n in range(BANKS):
                    cols = slice(n * BANK, (n + 1) * BANK)
                    last = pe.matmul(acc[:, cols], w, x[:, cols], start=start, stop=stop)
                return last

            def use(c, unit, acc, start=False, stop=False):
                kind, u = unit
                if unit in SPLIT:
                    pe.wait_ge(low_made, count(split, c, unit))
                    r, _ = place(split_pairs, PARTS, c, unit)
                    for e in range(PAIR):
                        w = SPLIT.index(unit) * PAIR + e
                        banks(acc, w_high[:, w, :], high[r][:, e, :], start and e == 0)
                        banks(acc, w_low[:, w, :], high[r][:, e, :])
                        last = banks(acc, w_high[:, w, :], low[r][:, e, :], stop=stop and e == PAIR - 1)
                else:
                    pe.wait_ge(unit_made, count(order, c, unit))
                    slot, _ = place(pairs, RING, c, unit)
                    w = (w0_sb if kind == "l0" else w1_sb)[:, u * PAIR:(u + 1) * PAIR, :]
                    for e in range(PAIR):
                        last = banks(acc, w[:, e, :], prod[slot][:, e, :], start and e == 0,
                                     stop and e == PAIR - 1)
                last.then_inc(unit_used, 1)

            def layer0(c):
                if not (isinstance(c[0], int) and number(c) == 0):
                    pe.wait_ge(acc0_free, number(c))
                use(c, ("l0", 0), acc0, start=True)
                use(c, ("l0", 1), acc0)
                pe.wait_ge(low_made, count(split, c, "rest"))
                banks(acc0, w0_rest_parts[:, :], rest_parts[:, :], stop=True).then_inc(unit_used, 1)

            def layer1(c, units):
                if units[0] == L1[0] and not is_first(c):
                    pe.wait_ge(acc1_free, number(c) - 1)
                for unit in units:
                    use(c, unit, acc1[c[1]], start=unit == L1[0], stop=unit == L1[-1])

            layer0((0, 0))

            def step(c):
                layer1(c, L1[:EARLY])
                layer0(after(c))
                layer1(c, L1[EARLY:])

            steps(pe, step, lambda c: layer1(c, L1))

            pe.wait_ge(top_w_in, 16 * 8)
            pe.wait_ge(acc0_free, CHUNKS)
            for n, (_, operands, _, _, m) in enumerate(top_groups()):
                if n == 0:
                    pe.wait_ge(acc1_free, CHUNKS - 1)
                if n == TOP1_GROUPS // HALVES:
                    pe.wait_ge(acc1_free, CHUNKS)
                if n >= 2:
                    pe.wait_ge(top_free, n - 1)
                if n == TOP1_GROUPS or n == TOP1_GROUPS + TOP2_GROUPS:
                    pe.wait_ge(top_free, n)
                for i, (w, x) in enumerate(operands):
                    last = pe.matmul(acc_top[n % 2][0:m, :], w, x, start=i == 0, stop=i == len(operands) - 1)
                last.then_inc(top_ready, 1)

        @block.scalar
        def _(act):
            act.dma_start(w0_sb[:, :, :], w0_im).then_inc(w0_in, 16)
            act.dma_start(w0_mi_sb[:, :, :], w0_mi).then_inc(w0_in, 16)
            act.dma_start(w0_rest_sb[:, :], w0_rest).then_inc(w0_in, 16)
            act.dma_start(w1_sb[:, :, :], w1).then_inc(w1_in, 16)
            act.dma_start(b0_sb[:, :], b0).then_inc(bias_in, 16)
            act.dma_start(b1_sb[:, :], b1).then_inc(bias_in, 16)

            def high_part(c, unit):
                r, last = place(split_pairs, PARTS, c, unit)
                if last:
                    act.wait_ge(unit_used, count(order, c, last[1], last[0]))
                act.wait_ge(unit_made, count(order, c, unit))
                slot, _ = place(pairs, RING, c, unit)
                act.activation(high[r][:, :, :], prod[slot][:, :, :], ACT.Copy).then_inc(high_made, 1)

            def high_rest(c):
                if not (isinstance(c[0], int) and number(c) == 0):
                    act.wait_ge(unit_used, count(order, c, "rest", 1))
                act.wait_ge(unit_made, count(order, c, "rest"))
                act.activation(rest_parts[0:FIELDS, :], rest[:, :], ACT.Copy)
                act.activation(rest_parts[FIELDS:2 * FIELDS, :], rest[:, :], ACT.Copy).then_inc(high_made, 1)

            def spread_h(c):
                p = c[1]
                act.wait_ge(unit_used, count(order, c, "rest"))
                if not is_first(c):
                    act.wait_ge(unit_made, count(order, c, L1[-1], back=2))
                for half in range(1 if isinstance(c[0], int) and number(c) == 0 else 2):
                    lo = HID + half * FIELDS
                    for g in range(GROUPS):
                        last = act.activation(h4[p][g * FIELDS:(g + 1) * FIELDS, half, :],
                                              acc0[lo:lo + FIELDS, :], ACT.Relu, bias=b0_sb[lo:lo + FIELDS, 0:1])
                last.then_inc(h_ready, 1)

            def sums(acc, bias, to, c, lo, hi):
                rows = acc.shape[0]
                for b in range(lo, hi):
                    part = acc[:, b * DIM:(b + 1) * DIM]
                    last = act.activation(part, part, ACT.Relu, bias=bias,
                                          accum_out=to[0:rows, bass.ds(number(c) * CHUNK + b, 1)])
                return last

            def sums0(c):
                sums(acc0[0:FEATS0, :], b0_sb[0:FEATS0, 0:1], feats0, c, 0, CHUNK).then_inc(acc0_free, 1)

            def sums1(c, lo=0, hi=CHUNK):
                if lo == 0:
                    act.wait_ge(unit_used, count(order, c, L1[-1]))
                last = sums(acc1[c[1]][:, :], b1_sb[:, 0:1], feats1, c, lo, hi)
                if hi == CHUNK:
                    last.then_inc(acc1_free, 1)

            act.wait_ge(w0_in, 48)
            act.activation(w0_rest_parts[0:FIELDS, :], w0_rest_sb[:, :], ACT.Copy)
            act.activation(w0_rest_parts[2 * FIELDS:, :], w0_rest_sb[:, :], ACT.Copy).then_inc(w_high_ready, 1)
            act.wait_ge(w0_ready, 3)
            act.wait_ge(w1_in, 16)
            for n, (kind, u) in enumerate(SPLIT):
                w = (w0_sb if kind == "l0" else w1_sb)[:, u * PAIR:(u + 1) * PAIR, :]
                act.activation(w_high[:, n * PAIR:(n + 1) * PAIR, :], w, ACT.Copy).then_inc(w_high_ready, 1)
            act.wait_ge(bias_in, 32)
            high_part((0, 0), ("l0", 1))
            high_rest((0, 0))
            spread_h((0, 0))
            sums0((0, 0))

            def step(c):
                high_part(c, ("l1", 1))
                started = isinstance(c[0], int) and number(c) == 0
                if not started:
                    sums1(before(c), 0, SUMS_EARLY)
                high_part(after(c), ("l0", 1))
                high_rest(after(c))
                high_part(c, ("l1", 2))
                if not started:
                    sums1(before(c), SUMS_EARLY, CHUNK)
                spread_h(after(c))
                sums0(after(c))

            def tail(c):
                high_part(c, ("l1", 1))
                high_part(c, ("l1", 2))
                sums1(before(c))
                sums1(c)

            steps(act, step, tail)
            act.wait_ge(top_w_in, 16 * 8)
            for n, (to, _, func, bias, m) in enumerate(top_groups()):
                act.wait_ge(top_ready, n + 1)
                if bias is None:
                    act.activation(to, acc_top[n % 2][0:m, :], func).then_inc(top_free, 1)
                else:
                    act.activation(to, acc_top[n % 2][0:m, :], func, bias=bias).then_inc(top_free, 1)


def kernel(**inputs):
    import concourse.bacc as bacc
    from concourse.bass_utils import run_bass_kernel_spmd

    a = {k: np.asarray(v) for k, v in inputs.items()}
    names = [f"tbl_{f}" for f in range(FIELDS)]
    tables = np.concatenate([a[n] for n in names], axis=0)
    starts = np.cumsum([0] + [a[n].shape[0] for n in names[:-1]]).astype(np.int32)

    ids = a["ids"].reshape(CHUNKS, GROUPS, PER_GROUP, FIELDS).transpose(1, 3, 0, 2).reshape(128, -1)
    base = np.tile(starts, GROUPS).reshape(128, 1)

    i = np.arange(FIELDS)
    order = np.r_[HID:OUTS, 0:HID]
    w0 = a["L0_rec_W0"].reshape(OUTS, FIELDS, FIELDS)[order]
    w1 = a["L0_rec_W1"].reshape(OUTS, 2, FIELDS, FIELDS)

    def tile0(w, swap):
        t = np.empty((GROUPS, FIELDS, FULL0, OUTS), w.dtype)
        for s in range(GROUPS * FULL0):
            m = (i + s) % FIELDS
            t[s % GROUPS, :, s // GROUPS, :] = (w[:, m, i] if swap else w[:, i, m]).T
        return t.reshape(128, FULL0, OUTS)

    t1 = np.empty((GROUPS, FIELDS, SHIFTS, 2, OUTS), w1.dtype)
    for s in range(FIELDS):
        for half in range(2):
            t1[s % GROUPS, :, s // GROUPS, half, :] = w1[:, half, i, (i + s) % FIELDS].T

    arrays = {
        "ids": ids, "table_base": base, "tables": tables, "dense": a["dense_ctx"].T,
        "w0_im": tile0(w0, False), "w0_mi": tile0(w0, True),
        "w0_rest": w0[:, i, (i + FIELDS // 2) % FIELDS].T, "b0": a["L0_rec_b0"][order].reshape(128, 1),
        "w1": t1.reshape(128, TILES1, OUTS), "b1": a["L0_rec_b1"].reshape(128, 1),
        "wt1": a["W_top1"], "bt1": a["b_top1"].reshape(-1, 128).T,
        "wt2": a["W_top2"].reshape(-1, 128, T2).transpose(1, 0, 2), "bt2": a["b_top2"].reshape(-1, 128).T,
        "wt3": a["W_top3"].reshape(-1, 128).T,
    }
    nc = bacc.Bacc("TRN2", target_bir_lowering=False, num_devices=1)
    arrays = {f"in_{k}": np.ascontiguousarray(v) for k, v in arrays.items()}
    args = [nc.dram_tensor(k, v.shape, mybir.dt.from_np(v.dtype), kind="ExternalInput").ap()
            for k, v in arrays.items()]
    out = nc.dram_tensor("out_y", (BATCH, 1), mybir.dt.float32, kind="ExternalOutput").ap()
    dlrm_tower(nc, *args, out)
    r = run_bass_kernel_spmd(nc, [arrays], core_ids=[0])
    return r.results[0]["out_y"]
```

```python
import numpy as np

import concourse.bass as bass
from concourse import mybir
from contextlib import ExitStack

FIELDS, DIM, BATCH, OUTS = 32, 64, 1024, 128
HID = OUTS // 2
GROUPS = 128 // FIELDS
CHUNK = 16
COLS = CHUNK * DIM
CHUNKS = BATCH // CHUNK
PER_GROUP = CHUNK // GROUPS
SHIFTS = FIELDS // GROUPS
FULL0 = FIELDS // 2 // GROUPS
TILES1 = 2 * SHIFTS
PAIR = 2
L0 = [("l0", 0), "squares", ("l0", 1)]
L1 = [("l1", u) for u in range(SHIFTS)]
FRONT = FULL0
EARLY = 2
SPLIT = {("l1", 0): 1, ("l1", 1): 2, ("l0", 1): 2, ("l1", 2): 2}
SPLIT_TILES = sum(SPLIT.values())
SPLIT_AT = {u: sum(list(SPLIT.values())[:n]) for n, u in enumerate(SPLIT)}
SUMS_EARLY = 6
RING = 5
PARTS = 2
BANK = 512
BANKS = COLS // BANK
T1, T2 = 512, 256
DENSE = 16
FEATS0 = OUTS - HID


def dlrm_tower(nc, ids, table_base, tables, dense, w0_im, w0_mi, w0_sq, b0, w1, b1,
               wt1, bt1, wt2, bt2, wt3, out):
    f32, f32r, i32 = mybir.dt.float32, mybir.dt.float32r, mybir.dt.int32
    ALU, ACT = mybir.AluOpType, mybir.ActivationFunctionType

    ctx = ExitStack()
    with ctx:
        def sb(name, shape, dt=f32):
            return ctx.enter_context(nc.sbuf_tensor(name, shape, dt))

        def ps(name, shape):
            return ctx.enter_context(nc.psum_tensor(name, shape, f32))

        def sem(name):
            return ctx.enter_context(nc.semaphore(name))

        x_dram = nc.dram_tensor("x_twice", [CHUNKS, 2, FIELDS, COLS], f32, kind="Internal").ap()

        ids_sb = sb("ids_sb", [128, CHUNKS * PER_GROUP], i32)
        base_sb = sb("base_sb", [128, 1], i32)
        rows_sb = [sb(f"rows_sb{p}", [128, PER_GROUP], i32) for p in range(2)]
        gath = [sb(f"gath{p}", [128, PER_GROUP * DIM]) for p in range(2)]
        x4 = [sb(f"x4_{p}", [128, COLS]) for p in range(2)]
        shifts = [sb(f"shifts{p}", [128, SHIFTS, COLS]) for p in range(2)]
        h4 = [sb(f"h4_{p}", [128, 2, COLS]) for p in range(2)]
        prod = [sb(f"prod{r}", [128, PAIR, COLS]) for r in range(RING)]
        high = [sb(f"high{r}", [128, PAIR, COLS], f32r) for r in range(PARTS)]
        low = [sb(f"low{r}", [128, PAIR, COLS], f32r) for r in range(PARTS)]
        squares = sb("squares", [FIELDS, COLS])
        squares_parts = sb("squares_parts", [3 * FIELDS, COLS], f32r)
        w0_sb = sb("w0_sb", [128, FULL0, OUTS])
        w0_mi_sb = sb("w0_mi_sb", [128, FULL0, OUTS])
        w0_sq_sb = sb("w0_sq_sb", [FIELDS, OUTS])
        w0_sq_parts = sb("w0_sq_parts", [3 * FIELDS, OUTS], f32r)
        w1_sb = sb("w1_sb", [128, TILES1, OUTS])
        w_high = sb("w_high", [128, SPLIT_TILES, OUTS], f32r)
        w_low = sb("w_low", [128, SPLIT_TILES, OUTS], f32r)
        b0_sb = sb("b0_sb", [128, 1])
        b1_sb = sb("b1_sb", [128, 1])
        feats0 = sb("feats0", [FEATS0 + DENSE, BATCH])
        feats1 = sb("feats1", [OUTS, BATCH])
        wt1_0 = sb("wt1_0", [FEATS0 + DENSE, T1])
        wt1_1 = sb("wt1_1", [OUTS, T1])
        bt1_sb = sb("bt1_sb", [128, T1 // 128])
        wt2_sb = sb("wt2_sb", [128, T1 // 128, T2])
        bt2_sb = sb("bt2_sb", [128, T2 // 128])
        wt3_sb = sb("wt3_sb", [128, T2 // 128])
        assert BATCH == COLS and T1 // 128 + T2 // 128 < SHIFTS
        top1 = shifts[0][:, 0:T1 // 128, :]
        top2 = shifts[0][:, T1 // 128:T1 // 128 + T2 // 128, :]
        y_sb = shifts[0][0:1, SHIFTS - 1, :]

        acc0 = ps("acc0", [128, COLS])
        acc1 = [ps(f"acc1_{p}", [128, COLS]) for p in range(2)]
        acc_top = [ps(f"acc_top{n}", [128, BANK]) for n in range(2)]
        acc_top += [acc0[:, n * BANK:(n + 1) * BANK] for n in range(BANKS)]
        TOPS = len(acc_top)

        ids_in = sem("ids_in")
        w0_in = sem("w0_in")
        w1_in = sem("w1_in")
        bias_in = sem("bias_in")
        top_w_in = sem("top_w_in")
        rows_ready = sem("rows_ready")
        w0_ready = sem("w0_ready")
        w_high_ready = sem("w_high_ready")
        w_low_ready = sem("w_low_ready")
        gathered = [sem(f"gathered{p}") for p in range(2)]
        stored = [sem(f"stored{p}") for p in range(2)]
        start_in = sem("start_in")
        front_in = [sem(f"front_in{p}") for p in range(2)]
        back_in = [sem(f"back_in{p}") for p in range(2)]
        unit_made = sem("unit_made")
        high_made = sem("high_made")
        low_made = sem("low_made")
        unit_used = sem("unit_used")
        acc0_free = sem("acc0_free")
        acc1_free = sem("acc1_free")
        h_ready = sem("h_ready")
        h1_ready = sem("h1_ready")
        top_ready = sem("top_ready")
        top_free = sem("top_free")
        y_out = sem("y_out")

        def number(c):
            return c[0] * 2 + c[1]

        def after(c):
            return (c[0], 1) if c[1] == 0 else (c[0] + 1, 0)

        def before(c):
            return (c[0], 0) if c[1] == 1 else (c[0] - 1, 1)

        order = [(0, u) for u in L0]
        for k in range(CHUNKS):
            order += [(k, u) for u in L1[:EARLY]]
            order += [(k + 1, u) for u in L0] if k + 1 < CHUNKS else []
            order += [(k, u) for u in L1[EARLY:]]
        pairs = [x for x in order if x[1] != "squares"]
        split = [x for x in order if x[1] in SPLIT or x[1] == "squares"]
        split_pairs = [x for x in order if x[1] in SPLIT]

        def count(units, c, unit, back=0):
            per = sum(1 for x in units if x[0] == 8)
            if isinstance(c[0], int):
                return units.index((number(c) - back, unit)) + 1
            k = 8 + c[1]
            return number(c) * per + (units.index((k - back, unit)) + 1 - k * per)

        def place(units, n, c, unit):
            k = number(c) if isinstance(c[0], int) else 8 + c[1]
            at = units.index((k, unit))
            return at % n, (k - units[at - n][0], units[at - n][1]) if at >= n else None

        def weights(unit, tiles):
            kind, u = unit
            return (w0_sb if kind == "l0" else w1_sb)[:, u * PAIR:u * PAIR + tiles, :]

        def split_weights(w, unit):
            return w[:, SPLIT_AT[unit]:SPLIT_AT[unit] + SPLIT[unit], :]

        def steps(engine, step, tail):
            for n in range(2):
                step((0, n))
            with engine.Fori(1, CHUNKS // 2 - 1) as half:
                for parity in range(2):
                    step((half, parity))
            step((CHUNKS // 2 - 1, 0))
            tail((CHUNKS // 2 - 1, 1))

        def is_zero(c):
            return isinstance(c[0], int) and number(c) == 0

        def is_first(c):
            return isinstance(c[0], int) and number(c) < 2

        def top_groups():
            halves = [slice(n * BANK, (n + 1) * BANK) for n in range(BATCH // BANK)]
            for h in halves:
                for m in range(T1 // 128):
                    cols = slice(m * 128, (m + 1) * 128)
                    yield (top1[:, m, h], [(wt1_0[:, cols], feats0[:, h]), (wt1_1[:, cols], feats1[:, h])],
                           ACT.Relu, bt1_sb[:, m:m + 1], 128)
            for h in halves:
                for m in range(T2 // 128):
                    cols = slice(m * 128, (m + 1) * 128)
                    yield (top2[:, m, h], [(wt2_sb[:, k, cols], top1[:, k, h]) for k in range(T1 // 128)],
                           ACT.Relu, bt2_sb[:, m:m + 1], 128)
            for h in halves:
                yield (y_sb[:, h], [(wt3_sb[:, k:k + 1], top2[:, k, h]) for k in range(T2 // 128)],
                       ACT.Copy, None, 1)

        HALVES = BATCH // BANK
        TOP1_GROUPS, TOP2_GROUPS = T1 // 128 * HALVES, T2 // 128 * HALVES
        LAYER2_END = TOP1_GROUPS + TOP2_GROUPS
        TOP_GROUPS = LAYER2_END + HALVES

        block = ctx.enter_context(nc.Block())

        @block.gpsimd
        def _(pool):
            pool.wait_ge(ids_in, 32)

            def gather(c):
                p = c[1]
                if not is_first(c):
                    pool.wait_ge(stored[p], c[0] * (16 * GROUPS))
                pool.tensor_tensor(rows_sb[p][:, :], ids_sb[:, bass.ds(number(c) * PER_GROUP, PER_GROUP)],
                                   base_sb[:, 0:1].to_broadcast([128, PER_GROUP]), ALU.add).then_inc(rows_ready, 1)
                pool.wait_ge(rows_ready, number(c) + 1)
                pool.nop(nofuse=True)
                for j in range(PER_GROUP):
                    pool.indirect_dma_start(
                        gath[p][:, j * DIM:(j + 1) * DIM], None, tables,
                        bass.IndirectOffsetOnAxis(ap=rows_sb[p][:, j:j + 1], axis=0),
                    ).then_inc(gathered[p], 16)

            steps(pool, gather, gather)

        @block.sync
        def _(sp):
            sp.dma_start(ids_sb[:, :], ids).then_inc(ids_in, 16)
            sp.dma_start(base_sb[:, :], table_base).then_inc(ids_in, 16)
            sp.dma_start(feats0[FEATS0:FEATS0 + DENSE, :], dense).then_inc(top_w_in, 16)

            def store(c):
                p = c[1]
                sp.wait_ge(gathered[p], c[0] * (16 * PER_GROUP) + 16 * PER_GROUP)
                w = PER_GROUP * DIM
                for g in range(GROUPS):
                    src = gath[p][g * FIELDS:(g + 1) * FIELDS, :].rearrange("f (a n) -> f a n", a=1)\
                        .to_broadcast([FIELDS, 2, w])
                    dst = x_dram[bass.ds(number(c), 1), :, :, g * w:(g + 1) * w].rearrange("a r f n -> (a f) r n")
                    sp.dma_start(dst, src).then_inc(stored[p], 16)

            def load(c):
                p = c[1]
                sp.wait_ge(stored[p], c[0] * (16 * GROUPS) + 16 * GROUPS)
                x = x_dram[bass.ds(number(c), 1), :, :, :].rearrange("a r f n -> (a r f) n")

                def shift_rows(g, lo, hi):
                    s = GROUPS * lo + g + 1
                    src = x[s:s + FIELDS, :]
                    rows = bass.AP(src.tensor, src.offset, [[COLS, FIELDS], [GROUPS * COLS, hi - lo], [1, COLS]])
                    return shifts[p][g * FIELDS:(g + 1) * FIELDS, lo:hi, :], rows

                if not is_first(c):
                    sp.wait_ge(unit_made, count(pairs, c, ("l1", FRONT - 1), back=2))
                zero = is_zero(c)
                for g in range(GROUPS):
                    sp.dma_start(x4[p][g * FIELDS:(g + 1) * FIELDS, :], x[0:FIELDS, :])\
                        .then_inc(start_in if zero else front_in[p], 16)
                if zero:
                    pieces = ((0, PAIR, start_in), (PAIR, PAIR + 1, front_in[p]), (PAIR + 1, FRONT, front_in[p]))
                    for lo, hi, done in pieces:
                        for g in range(GROUPS):
                            sp.dma_start(*shift_rows(g, lo, hi)).then_inc(done, 16)
                else:
                    for g in range(GROUPS):
                        sp.dma_start(*shift_rows(g, 0, FRONT)).then_inc(front_in[p], 16)
                if not is_first(c):
                    sp.wait_ge(unit_made, count(pairs, c, L1[-1], back=2))
                for g in range(GROUPS):
                    sp.dma_start(*shift_rows(g, FRONT, SHIFTS)).then_inc(back_in[p], 16)

            store((0, 0))
            load((0, 0))

            def step(c):
                store(after(c))
                if not is_zero(c):
                    load(c)

            steps(sp, step, load)
            sp.dma_start(wt1_0[0:FEATS0, :], wt1[0:FEATS0, :]).then_inc(top_w_in, 16)
            sp.dma_start(wt1_0[FEATS0:FEATS0 + DENSE, :], wt1[FEATS0 + OUTS:, :]).then_inc(top_w_in, 16)
            sp.dma_start(wt1_1[:, :], wt1[FEATS0:FEATS0 + OUTS, :]).then_inc(top_w_in, 16)
            sp.dma_start(wt2_sb[:, :, :], wt2).then_inc(top_w_in, 16)
            sp.dma_start(wt3_sb[:, :], wt3).then_inc(top_w_in, 16)
            sp.dma_start(bt1_sb[:, :], bt1).then_inc(top_w_in, 16)
            sp.dma_start(bt2_sb[:, :], bt2).then_inc(top_w_in, 16)
            sp.wait_ge(top_free, TOP_GROUPS)
            sp.dma_start(out.rearrange("b a -> a b"), y_sb).then_inc(y_out, 16)
            sp.wait_ge(y_out, 16)

        @block.vector
        def _(dve):
            def product(c, unit):
                p = c[1]
                kind, u = unit
                zero = is_zero(c)
                if kind == "l0" and zero and u == 0:
                    dve.wait_ge(start_in, 16 * 2 * GROUPS)
                elif kind == "l0" and u == (1 if zero else 0):
                    dve.wait_ge(front_in[p], c[0] * (16 * 2 * GROUPS) + 16 * 2 * GROUPS)
                if kind == "l1" and u == 0:
                    dve.wait_ge(h_ready, number(c) + 1)
                if kind == "l1" and u == FRONT:
                    dve.wait_ge(back_in[p], c[0] * (16 * GROUPS) + 16 * GROUPS)
                slot, last = place(pairs, RING, c, unit)
                if last and SPLIT.get(last[1]) == PAIR:
                    dve.wait_ge(low_made, count(split, c, last[1], last[0]))
                elif last:
                    dve.wait_ge(unit_used, count(order, c, last[1], last[0]))
                if kind == "l0":
                    a = x4[p][:, :].rearrange("p (a n) -> p a n", a=1).to_broadcast([128, PAIR, COLS])
                    b = shifts[p][:, u * PAIR:(u + 1) * PAIR, :]
                else:
                    a = h4[p][:, :, :]
                    b = shifts[p][:, u:u + 1, :].to_broadcast([128, PAIR, COLS])
                dve.tensor_tensor(prod[slot][:, :, :], a, b, ALU.mult).then_inc(unit_made, 1)

            def low_part(c, unit):
                dve.wait_ge(high_made, count(split, c, unit))
                slot, _ = place(pairs, RING, c, unit)
                r, _ = place(split_pairs, PARTS, c, unit)
                n = SPLIT[unit]
                dve.tensor_tensor(low[r][:, 0:n, :], prod[slot][:, 0:n, :], high[r][:, 0:n, :].bitcast(f32),
                                  ALU.subtract).then_inc(low_made, 1)

            def low_squares(c):
                dve.wait_ge(high_made, count(split, c, "squares"))
                """squares - their high parts."""
                dve.tensor_tensor(squares_parts[2 * FIELDS:, :], squares[:, :],
                                  squares_parts[0:FIELDS, :].bitcast(f32), ALU.subtract).then_inc(low_made, 1)

            dve.wait_ge(w0_in, 48)
            for lo, hi, t0, t1 in ((0, 128, 0, FULL0 - 1), (0, 2 * FIELDS, FULL0 - 1, FULL0),
                                   (2 * FIELDS, 3 * FIELDS, FULL0 - 1, FULL0)):
                part = w0_sb[lo:hi, t0:t1, :]
                dve.tensor_tensor(part, part, w0_mi_sb[lo:hi, t0:t1, :], ALU.add).then_inc(w0_ready, 1)
            dve.wait_ge(w_high_ready, 1)
            dve.tensor_tensor(w0_sq_parts[FIELDS:2 * FIELDS, :], w0_sq_sb[:, :],
                              w0_sq_parts[0:FIELDS, :].bitcast(f32), ALU.subtract).then_inc(w_low_ready, 1)
            for n, unit in enumerate(SPLIT):
                dve.wait_ge(w_high_ready, n + 2)
                dve.tensor_tensor(split_weights(w_low, unit), weights(unit, SPLIT[unit]),
                                  split_weights(w_high, unit).bitcast(f32), ALU.subtract).then_inc(w_low_ready, 1)
            product((0, 0), ("l0", 0))
            product((0, 0), ("l0", 1))
            low_squares((0, 0))
            low_part((0, 0), ("l0", 1))
            dve.wait_ge(bias_in, 32)
            dve.wait_ge(unit_used, count(order, (0, 0), L0[-1]))
            for g in range(GROUPS):
                dve.tensor_scalar(h4[0][g * FIELDS:(g + 1) * FIELDS, 1, :], acc0[OUTS - FIELDS:OUTS, :],
                                  b0_sb[OUTS - FIELDS:OUTS, 0:1], 0.0, ALU.add, ALU.max).then_inc(h1_ready, 1)
            dve.wait_ge(h1_ready, GROUPS)

            def step(c):
                product(c, ("l1", 0))
                product(c, ("l1", 1))
                product(after(c), ("l0", 0))
                low_part(c, ("l1", 0))
                low_part(c, ("l1", 1))
                product(after(c), ("l0", 1))
                low_squares(after(c))
                product(c, ("l1", 2))
                low_part(after(c), ("l0", 1))
                product(c, ("l1", 3))
                low_part(c, ("l1", 2))
                for u in range(4, SHIFTS):
                    product(c, ("l1", u))

            def tail(c):
                product(c, ("l1", 0))
                product(c, ("l1", 1))
                low_part(c, ("l1", 0))
                product(c, ("l1", 2))
                low_part(c, ("l1", 1))
                product(c, ("l1", 3))
                low_part(c, ("l1", 2))
                for u in range(4, SHIFTS):
                    product(c, ("l1", u))

            steps(dve, step, tail)

        @block.tensor
        def _(pe):
            pe.wait_ge(w0_in, 48)
            pe.wait_ge(w1_in, 16)
            pe.wait_ge(w0_ready, 3)
            pe.wait_ge(w_low_ready, 1 + len(SPLIT))

            def banks(acc, w, x, start=False, stop=False):
                for n in range(BANKS):
                    cols = slice(n * BANK, (n + 1) * BANK)
                    last = pe.matmul(acc[:, cols], w, x[:, cols], start=start, stop=stop)
                return last

            def use(c, unit, acc, start=False, stop=False):
                n = SPLIT.get(unit, 0)
                slot, _ = place(pairs, RING, c, unit)
                if n:
                    pe.wait_ge(low_made, count(split, c, unit))
                    r, _ = place(split_pairs, PARTS, c, unit)
                else:
                    pe.wait_ge(unit_made, count(pairs, c, unit))
                for e in range(PAIR):
                    first, end = start and e == 0, stop and e == PAIR - 1
                    if e < n:
                        w_h, w_l = split_weights(w_high, unit)[:, e, :], split_weights(w_low, unit)[:, e, :]
                        banks(acc, w_h, high[r][:, e, :], first)
                        banks(acc, w_l, high[r][:, e, :])
                        last = banks(acc, w_h, low[r][:, e, :], stop=end)
                    else:
                        last = banks(acc, weights(unit, PAIR)[:, e, :], prod[slot][:, e, :], first, end)
                last.then_inc(unit_used, 1)

            def layer0(c):
                if not is_zero(c):
                    pe.wait_ge(acc0_free, number(c))
                use(c, ("l0", 0), acc0, start=True)
                pe.wait_ge(low_made, count(split, c, "squares"))
                banks(acc0, w0_sq_parts[:, :], squares_parts[:, :]).then_inc(unit_used, 1)
                use(c, ("l0", 1), acc0, stop=True)

            def layer1(c, units):
                if units[0] == L1[0] and not is_first(c):
                    pe.wait_ge(acc1_free, number(c) - 1)
                for unit in units:
                    use(c, unit, acc1[c[1]], start=unit == L1[0], stop=unit == L1[-1])

            layer0((0, 0))

            def step(c):
                layer1(c, L1[:EARLY])
                layer0(after(c))
                layer1(c, L1[EARLY:])

            steps(pe, step, lambda c: layer1(c, L1))

            pe.wait_ge(top_w_in, 16 * 8)
            pe.wait_ge(acc0_free, CHUNKS)
            for n, (_, operands, _, _, m) in enumerate(top_groups()):
                if n == 0:
                    pe.wait_ge(acc1_free, CHUNKS - 1)
                if n == TOP1_GROUPS // HALVES:
                    pe.wait_ge(acc1_free, CHUNKS)
                if n >= TOPS:
                    pe.wait_ge(top_free, n - TOPS + 1)
                for width, lo, hi in ((TOP2_GROUPS // HALVES, 0, TOP1_GROUPS), (1, TOP1_GROUPS, LAYER2_END)):
                    if n >= hi and (n - hi) % width == 0 and (n - hi) // width < HALVES:
                        pe.wait_ge(top_free, lo + ((n - hi) // width + 1) * (hi - lo) // HALVES)
                for i, (w, x) in enumerate(operands):
                    last = pe.matmul(acc_top[n % TOPS][0:m, :], w, x, start=i == 0, stop=i == len(operands) - 1)
                last.then_inc(top_ready, 1)

        @block.scalar
        def _(act):
            act.dma_start(w0_sb[:, :, :], w0_im).then_inc(w0_in, 16)
            act.dma_start(w0_mi_sb[:, :, :], w0_mi).then_inc(w0_in, 16)
            act.dma_start(w0_sq_sb[:, :], w0_sq).then_inc(w0_in, 16)
            act.dma_start(w1_sb[:, :, :], w1).then_inc(w1_in, 16)
            act.dma_start(b0_sb[:, :], b0).then_inc(bias_in, 16)
            act.dma_start(b1_sb[:, :], b1).then_inc(bias_in, 16)

            def high_part(c, unit):
                r, last = place(split_pairs, PARTS, c, unit)
                if last:
                    act.wait_ge(unit_used, count(order, c, last[1], last[0]))
                act.wait_ge(unit_made, count(pairs, c, unit))
                slot, _ = place(pairs, RING, c, unit)
                n = SPLIT[unit]
                act.activation(high[r][:, 0:n, :], prod[slot][:, 0:n, :], ACT.Copy).then_inc(high_made, 1)

            def square(c):
                p = c[1]
                if is_zero(c):
                    act.wait_ge(start_in, 16 * 2 * GROUPS)
                else:
                    act.wait_ge(front_in[p], c[0] * (16 * 2 * GROUPS) + 16 * 2 * GROUPS)
                    act.wait_ge(unit_used, count(order, c, "squares", 1))
                x = x4[p][0:FIELDS, :]
                act.activation(squares[:, :], x, ACT.Square)
                act.activation(squares_parts[0:FIELDS, :], x, ACT.Square)
                act.activation(squares_parts[FIELDS:2 * FIELDS, :], x, ACT.Square).then_inc(high_made, 1)

            def spread_h(c):
                p = c[1]
                act.wait_ge(unit_used, count(order, c, L0[-1]))
                if not is_first(c):
                    act.wait_ge(unit_made, count(pairs, c, L1[-1], back=2))
                for half in range(1 if is_zero(c) else 2):
                    lo = HID + half * FIELDS
                    for g in range(GROUPS):
                        last = act.activation(h4[p][g * FIELDS:(g + 1) * FIELDS, half, :],
                                              acc0[lo:lo + FIELDS, :], ACT.Relu,
                                              bias=b0_sb[lo:lo + FIELDS, 0:1])
                last.then_inc(h_ready, 1)

            def sums(acc, bias, to, c, lo, hi):
                rows = acc.shape[0]
                for b in range(lo, hi):
                    part = acc[:, b * DIM:(b + 1) * DIM]
                    last = act.activation(part, part, ACT.Relu, bias=bias,
                                          accum_out=to[0:rows, bass.ds(number(c) * CHUNK + b, 1)])
                return last

            def sums0(c):
                sums(acc0[0:FEATS0, :], b0_sb[0:FEATS0, 0:1], feats0, c, 0, CHUNK).then_inc(acc0_free, 1)

            def sums1(c, lo=0, hi=CHUNK):
                if lo == 0:
                    act.wait_ge(unit_used, count(order, c, L1[-1]))
                last = sums(acc1[c[1]][:, :], b1_sb[:, 0:1], feats1, c, lo, hi)
                if hi == CHUNK:
                    last.then_inc(acc1_free, 1)

            act.wait_ge(w0_in, 48)
            act.activation(w0_sq_parts[0:FIELDS, :], w0_sq_sb[:, :], ACT.Copy)
            act.activation(w0_sq_parts[2 * FIELDS:, :], w0_sq_sb[:, :], ACT.Copy).then_inc(w_high_ready, 1)
            act.wait_ge(w0_ready, 3)
            act.wait_ge(w1_in, 16)
            for unit in SPLIT:
                act.activation(split_weights(w_high, unit), weights(unit, SPLIT[unit]), ACT.Copy)\
                    .then_inc(w_high_ready, 1)
            act.wait_ge(bias_in, 32)
            square((0, 0))
            high_part((0, 0), ("l0", 1))
            spread_h((0, 0))
            sums0((0, 0))

            def step(c):
                high_part(c, ("l1", 0))
                high_part(c, ("l1", 1))
                square(after(c))
                if not is_zero(c):
                    sums1(before(c), 0, SUMS_EARLY)
                high_part(after(c), ("l0", 1))
                high_part(c, ("l1", 2))
                if not is_zero(c):
                    sums1(before(c), SUMS_EARLY, CHUNK)
                spread_h(after(c))
                sums0(after(c))

            def tail(c):
                high_part(c, ("l1", 0))
                high_part(c, ("l1", 1))
                high_part(c, ("l1", 2))
                sums1(before(c))
                sums1(c)

            steps(act, step, tail)
            act.wait_ge(top_w_in, 16 * 8)
            for n, (to, _, func, bias, m) in enumerate(top_groups()):
                act.wait_ge(top_ready, n + 1)
                if bias is None:
                    act.activation(to, acc_top[n % TOPS][0:m, :], func).then_inc(top_free, 1)
                else:
                    act.activation(to, acc_top[n % TOPS][0:m, :], func, bias=bias).then_inc(top_free, 1)


def kernel(**inputs):
    import concourse.bacc as bacc
    from concourse.bass_utils import run_bass_kernel_spmd

    a = {k: np.asarray(v) for k, v in inputs.items()}
    names = [f"tbl_{f}" for f in range(FIELDS)]
    tables = np.concatenate([a[n] for n in names], axis=0)
    starts = np.cumsum([0] + [a[n].shape[0] for n in names[:-1]]).astype(np.int32)

    ids = a["ids"].reshape(CHUNKS, GROUPS, PER_GROUP, FIELDS).transpose(1, 3, 0, 2).reshape(128, -1)
    base = np.tile(starts, GROUPS).reshape(128, 1)

    i = np.arange(FIELDS)
    order = np.r_[HID:OUTS, 0:HID]
    w0 = a["L0_rec_W0"].reshape(OUTS, FIELDS, FIELDS)[order]
    w1 = a["L0_rec_W1"].reshape(OUTS, 2, FIELDS, FIELDS)

    def tile0(w, swap):
        t = np.empty((GROUPS, FIELDS, FULL0, OUTS), w.dtype)
        for s in range(GROUPS * FULL0):
            m = (i + s + 1) % FIELDS
            t[s % GROUPS, :, s // GROUPS, :] = (w[:, m, i] if swap else w[:, i, m]).T
        return t.reshape(128, FULL0, OUTS)

    t1 = np.empty((GROUPS, FIELDS, SHIFTS, 2, OUTS), w1.dtype)
    for s in range(FIELDS):
        for half in range(2):
            t1[s % GROUPS, :, s // GROUPS, half, :] = w1[:, half, i, (i + s + 1) % FIELDS].T

    arrays = {
        "ids": ids, "table_base": base, "tables": tables, "dense": a["dense_ctx"].T,
        "w0_im": tile0(w0, False), "w0_mi": tile0(w0, True),
        "w0_sq": w0[:, i, i].T, "b0": a["L0_rec_b0"][order].reshape(128, 1),
        "w1": t1.reshape(128, TILES1, OUTS), "b1": a["L0_rec_b1"].reshape(128, 1),
        "wt1": a["W_top1"], "bt1": a["b_top1"].reshape(-1, 128).T,
        "wt2": a["W_top2"].reshape(-1, 128, T2).transpose(1, 0, 2), "bt2": a["b_top2"].reshape(-1, 128).T,
        "wt3": a["W_top3"].reshape(-1, 128).T,
    }
    nc = bacc.Bacc("TRN2", target_bir_lowering=False, num_devices=1)
    arrays = {f"in_{k}": np.ascontiguousarray(v) for k, v in arrays.items()}
    args = [nc.dram_tensor(k, v.shape, mybir.dt.from_np(v.dtype), kind="ExternalInput").ap()
            for k, v in arrays.items()]
    out = nc.dram_tensor("out_y", (BATCH, 1), mybir.dt.float32, kind="ExternalOutput").ap()
    dlrm_tower(nc, *args, out)
    r = run_bass_kernel_spmd(nc, [arrays], core_ids=[0])
    return r.results[0]["out_y"]
```
